# Optimizing a Trainium2 kernel written in Bass

```python
import numpy as np
import jax
import jax.numpy as jnp

def _softmax(x, axis=-1):
    return jax.nn.softmax(x, axis=axis)

def _gelu(x):
    return jax.nn.gelu(x, approximate=True)

def _silu(x):
    return jax.nn.silu(x)

def _sigmoid(x):
    return jax.nn.sigmoid(x)

def _layernorm(x, axis=-1, eps=1e-05):
    m = jnp.mean(x, axis=axis, keepdims=True)
    v = jnp.var(x, axis=axis, keepdims=True)
    return (x - m) / jnp.sqrt(v + eps)

def _scatter_add(tgt, idx, src, axis=0):
    return tgt.at[idx].add(src)

def _segment_sum(src, seg, n):
    return jax.ops.segment_sum(src, seg, n)
kernel_name = 'mk_gnn_preln_d1_gnn_r64_dbebd1'

def setup_inputs(seed: int=0):
    np.random.seed(seed)
    _w = jnp.asarray

    def _rec_inputs():
        import jax
        import jax.numpy as jnp
        _gk = jax.random.key(seed)
        x = -8.776e-05 + 1 * jax.random.normal(jax.random.fold_in(_gk, 1), (50000, 512), jnp.float32)
        src = jax.random.randint(jax.random.fold_in(_gk, 2), (12500,), 0, 50000, jnp.int32)
        dst = jnp.minimum((50000 * jax.random.uniform(jax.random.fold_in(_gk, 3), (12500,)) ** 2.0).astype(jnp.int32), 49999)
        _o = jnp.argsort(dst, stable=True)
        src = src[_o]
        dst = dst[_o]
        return (x, src, dst)
    x, src, dst = _rec_inputs()

    def _L0_gnn_setup():
        import jax, jax.numpy as jnp
        import numpy as np
        N_NODES = 10000
        N_EDGES = 2500
        D_FEAT = 512
        OUT_CH = 512
        key = jax.random.key(seed)
        k1, k2, k3, k4 = jax.random.split(key, 4)
        x = jax.random.normal(k1, (N_NODES, D_FEAT), dtype=jnp.float32)
        edge_index = jax.random.randint(k2, (N_EDGES, 2), 0, N_NODES, dtype=jnp.int64)
        W = jax.random.normal(k3, (OUT_CH, 2 * D_FEAT), dtype=jnp.float32) / np.sqrt(2 * D_FEAT)
        b = jax.random.normal(k4, (OUT_CH,), dtype=jnp.float32) * 0.01
        return {'x': x, 'edge_index': edge_index, 'num_local_nodes': N_NODES, 'W': W, 'b': b}
    _L0_gnn_all = _L0_gnn_setup()
    _L0_gnn_in = {k: v for k, v in _L0_gnn_all.items() if k in ('W', 'b')}
    del _L0_gnn_all
    return {'x': x, 'src': src, 'dst': dst, 'L0_gnn_W': _L0_gnn_in['W'], 'L0_gnn_b': _L0_gnn_in['b']}

def reference(x, src, dst, L0_gnn_W, L0_gnn_b):
    import jax
    import jax.numpy as jnp

    def _L0_gnn_ref(x, edge_index, num_local_nodes, W, b):
        import jax, jax.numpy as jnp
        import numpy as np
        N_NODES = 10000
        N_EDGES = 2500
        D_FEAT = 512
        OUT_CH = 512
        src = edge_index[:, 0]
        tgt = edge_index[:, 1]
        x_i = x[src]
        x_j = x[tgt]
        x_ij = jnp.concatenate([x_i, x_j], axis=1)
        m_ij = jax.nn.relu(x_ij @ W.T + b)
        out = jax.ops.segment_sum(m_ij, src, num_segments=num_local_nodes)
        return out
    edge_index_t = jnp.stack([src, dst], axis=1)
    h = jnp.maximum(_layernorm(x, axis=-1), 0.0)
    x = x + _L0_gnn_ref(h, edge_index_t, 50000, L0_gnn_W, L0_gnn_b)
    return x

_drawn_inputs = setup_inputs


def setup_inputs(seed=0):
    import zlib

    import numpy as np

    out = dict(_drawn_inputs(seed))
    spreads = {}
    factors = {'L0_gnn_b': 8.0}
    for name, (base, spread) in spreads.items():
        noise = np.random.default_rng([zlib.crc32(name.encode()), seed]).standard_normal(out[name].shape)
        drawn = base * np.exp(spread * noise) if base else spread * noise
        out[name] = jnp.asarray(drawn.astype(out[name].dtype))
    for name, factor in factors.items():
        out[name] = (out[name] * factor).astype(out[name].dtype)
    return out
```

```python
import concourse.bass as bass
from concourse import mybir
from contextlib import ExitStack


def gnn_message_passing_kernel(
    nc: bass.Bass,
    x: bass.AP,
    src_cols: bass.AP,
    src_rows: bass.AP,
    dst_cols: bass.AP,
    w_t: bass.AP,
    bias: bass.AP,
    out: bass.AP,
):
    F32 = mybir.dt.float32
    F32R = mybir.dt.float32r
    I32 = mybir.dt.int32
    ALU = mybir.AluOpType
    ACT = mybir.ActivationFunctionType

    P = 128
    N, D = x.shape
    TILES = src_cols.shape[1]
    OUT = w_t.shape[1]
    SIDES = 2
    KD = D // P
    K = SIDES * KD
    EPS = 1e-5
    RING = 53
    FIRST_ADD = 46
    ADDS_PER_GATHER = 2
    COPY_ROWS = 2000
    COPIES = N // COPY_ROWS
    COPY_RUNS = 80
    assert N % COPY_ROWS == 0 and TILES % 4 == 2 and RING % 4 == 1 and OUT == D and D == 512
    assert FIRST_ADD <= RING < TILES - 4

    ctx = ExitStack()
    with ctx:
        def sb(name, shape, dt):
            return ctx.enter_context(nc.sbuf_tensor(name, shape, dt))

        def ps(name, shape):
            return ctx.enter_context(nc.psum_tensor(name, shape, F32))

        def sem(name):
            return ctx.enter_context(nc.semaphore(name))

        w_hi = sb("w_hi", [P, K, OUT], F32R)
        w_lo = sb("w_lo", [P, K, OUT], F32R)
        bias_bc = sb("bias_bc", [P, OUT], F32)
        src_i = sb("src_i", [P, TILES], I32)
        dst_i = sb("dst_i", [P, TILES], I32)
        src_f = sb("src_f", [P, TILES], F32)
        spare_i = sb("spare_i", [P, 1], I32)
        spare_f = sb("spare_f", [P, 1], F32)
        to_spare = sb("to_spare", [P, TILES], F32)
        identity = sb("identity", [P, P], F32)
        earlier = sb("earlier", [P, P], F32)
        eps = sb("eps", [P, 1], F32)
        add_i = sb("add_i", [P, TILES], I32)
        xg = sb("xg", [P, 2, SIDES, D], F32)
        stats = sb("stats", [P, 2, SIDES, 6], F32)
        mean_var = sb("mean_var", [P, 2, SIDES, 2], F32)
        std = sb("std", [P, 2, SIDES], F32)
        rstd = sb("rstd", [P, 2, SIDES], F32)
        shift = sb("shift", [P, 2, SIDES], F32)
        h = sb("h", [P, 2, SIDES, D], F32)
        ht_hi = sb("ht_hi", [P, 2, SIDES, KD * P], F32R)
        ht_lo = sb("ht_lo", [P, 2, SIDES, KD * P], F32R)
        src_row = sb("src_row", [P, 2, 2 * P], I32)
        same = sb("same", [P, 2, P], F32R)
        found = sb("found", [P, 2, P], F32)
        count = sb("count", [P, 2], F32)
        move = sb("move", [P, 2], F32)
        zb = sb("zb", [P, 2, OUT], F32)
        m_hi = sb("m_hi", [P, 2, OUT], F32R)
        m_lo = sb("m_lo", [P, 2, OUT], F32R)
        ring = sb("ring", [P, RING, OUT], F32)

        ht_ps = [[ps(f"ht_ps{b}{s}", [P, KD * P]) for s in range(SIDES)] for b in range(2)]
        z_ps = [ps(f"z_ps{b}", [P, OUT]) for b in range(2)]
        agg_ps = [ps(f"agg_ps{b}", [P, OUT]) for b in range(2)]

        src_loaded = sem("src_loaded")
        dst_loaded = sem("dst_loaded")
        w_loaded = sem("w_loaded")
        bias_loaded = sem("bias_loaded")
        copied = sem("copied")
        consts = sem("consts")
        eps_made = sem("eps_made")
        spare_made = sem("spare_made")
        x_arrived = [sem(f"x_arrived{b}") for b in range(2)]
        row_arrived = [sem(f"row_arrived{b}") for b in range(2)]
        scattered = sem("scattered")
        src_cast = sem("src_cast")
        w_hi_ready = sem("w_hi_ready")
        w_lo_ready = sem("w_lo_ready")
        stats_done = sem("stats_done")
        var_ready = sem("var_ready")
        std_ready = sem("std_ready")
        rstd_done = sem("rstd_done")
        norm_ready = sem("norm_ready")
        h_ready = sem("h_ready")
        transposed = sem("transposed")
        hi_ready = sem("hi_ready")
        lo_ready = sem("lo_ready")
        mm_done = sem("mm_done")
        biased = sem("biased")
        mhi_ready = sem("mhi_ready")
        mlo_ready = sem("mlo_ready")
        same_ready = sem("same_ready")
        counted = sem("counted")
        moved = sem("moved")
        add_ready = sem("add_ready")
        agg_done = sem("agg_done")
        ring_filled = sem("ring_filled")

        block = ctx.enter_context(nc.Block())

        @block.sync
        def _(sp):
            sp.dma_start(dst_i[:, :], dst_cols).then_inc(dst_loaded, 16)
            sp.dma_start(src_i[:, :], src_cols).then_inc(src_loaded, 16)
            sp.dma_start(ring[:, 0:K, :], w_t.rearrange("(k p) o -> p k o", p=P)).then_inc(w_loaded, 16)
            sp.dma_start(bias_bc[:, :], bias.to_broadcast([P, OUT])).then_inc(bias_loaded, 16)
            sp.dma_start(out[N:N + P, :], x[0:P, :]).then_inc(copied, 16)
            out_runs = out[0:N, :].rearrange("(c a b) d -> c a (b d)", a=COPY_RUNS, c=COPIES)
            x_runs = x.rearrange("(c a b) d -> c a (b d)", a=COPY_RUNS, c=COPIES)
            with sp.Fori(0, COPIES) as c:
                sp.dma_start(out_runs[c], x_runs[c]).then_inc(copied, 16)

        @block.gpsimd
        def _(pool):
            def gather(t):
                b = t % 2
                if t >= 2:
                    pool.wait_ge(h_ready, SIDES * (t - 1))
                for s, (nodes, loaded) in enumerate(((src_i, src_loaded), (dst_i, dst_loaded))):
                    if t == 0:
                        pool.wait_ge(loaded, 16)
                    nc.gpsimd.indirect_dma_start(
                        out=xg[:, b, s, :], out_offset=None, in_=x,
                        in_offset=bass.IndirectOffsetOnAxis(ap=nodes[:, t:t + 1], axis=0),
                        bounds_check=N - 1, oob_is_err=False).then_inc(x_arrived[b], 16)

            def add(t):
                if t == 0:
                    pool.wait_ge(copied, 16 * (COPIES + 1))
                else:
                    pool.wait_ge(scattered, 16 * t)
                pool.wait_ge(add_ready, t + 1)
                pool.wait_ge(ring_filled, t + 1)
                nc.gpsimd.indirect_dma_start(
                    out=out, out_offset=bass.IndirectOffsetOnAxis(ap=add_i[:, t:t + 1], axis=0),
                    in_=ring[:, t % RING, :], in_offset=None, bounds_check=N + P - 1,
                    compute_op=ALU.add).then_inc(scattered, 16)

            gather(0)
            gather(1)
            nc.gpsimd.iota(spare_i[:, :], pattern=[[0, 1]], base=N, channel_multiplier=1).then_inc(spare_made, 1)
            nc.gpsimd.memset(eps[:, :], EPS).then_inc(eps_made, 1)
            nc.gpsimd.memset(identity[:, :], 0.0).then_inc(consts, 1)
            nc.gpsimd.memset(earlier[:, :], 1.0).then_inc(consts, 1)
            pool.wait_ge(consts, 2)
            nc.gpsimd.affine_select(out=identity[:, :], in_=identity[:, :], compare_op=ALU.not_equal, fill=1.0,
                                    base=0, pattern=[[-1, P]], channel_multiplier=1).then_inc(consts, 1)
            nc.gpsimd.affine_select(out=earlier[:, :], in_=earlier[:, :], compare_op=ALU.is_gt, fill=0.0,
                                    base=0, pattern=[[-1, P]], channel_multiplier=1).then_inc(consts, 1)
            for t in range(2, FIRST_ADD):
                gather(t)
            added = 0
            for t in range(FIRST_ADD, TILES):
                for _ in range(ADDS_PER_GATHER):
                    if added < t - 6:
                        add(added)
                        added += 1
                gather(t)
            for t in range(added, TILES):
                add(t)
            pool.wait_ge(scattered, 16 * TILES)

        @block.vector
        def _(dve):
            def statistics(t, b):
                dve.wait_ge(x_arrived[b], 16 * (t - b) + 32)
                for s in range(SIDES):
                    nc.vector.bn_stats(stats[:, b, s, :], xg[:, b, s, :]).then_inc(stats_done, 1)

            def aggregate(t, b):
                if isinstance(t, int):
                    dve.wait_ge(stats_done, SIDES * (t + 1))
                for s in range(SIDES):
                    nc.vector.bn_aggr(mean_var[:, b, s, :], stats[:, b, s, :]).then_inc(var_ready, 1)

            def scales(t, b):
                dve.wait_ge(std_ready, t + 1)
                nc.vector.reciprocal(rstd[:, b, :], std[:, b, :]).then_inc(rstd_done, 1)
                dve.wait_ge(rstd_done, t + 1)
                nc.vector.scalar_tensor_tensor(out=shift[:, b, :], in0=mean_var[:, b, :, 0], scalar=-1.0,
                                               in1=rstd[:, b, :], op0=ALU.mult, op1=ALU.mult
                                               ).then_inc(norm_ready, 1)

            def low_parts(t, b):
                for s in range(SIDES):
                    dve.wait_ge(hi_ready, SIDES * t + s + 1)
                    nc.vector.tensor_tensor(ht_lo[:, b, s, :], ht_ps[b][s][:, :], ht_hi[:, b, s, :].bitcast(F32),
                                            ALU.subtract).then_inc(lo_ready, 1)

            def add_bias(t, b):
                dve.wait_ge(mm_done, t + 1)
                nc.vector.tensor_tensor(zb[:, b, :], z_ps[b][:, :], bias_bc[:, :], ALU.add).then_inc(biased, 1)

            def same_source(t, b, pair_slot):
                dve.wait_ge(row_arrived[pair_slot], 4 * (t - b - 2 * pair_slot) + 16)
                if not (isinstance(t, int) and t < 2):
                    dve.wait_ge(agg_done, t - 1)
                row = src_row[:, pair_slot, b * P:(b + 1) * P]
                mine = src_f[:, bass.ds(t, 1)]
                nc.vector.tensor_scalar(same[:, b, :], row, mine, None, ALU.is_equal).then_inc(same_ready, 1)
                nc.vector.scalar_tensor_tensor(out=found[:, b, :], in0=row, scalar=mine, in1=earlier[:, :],
                                               op0=ALU.is_equal, op1=ALU.mult, accum_out=count[:, b:b + 1]
                                               ).then_inc(counted, 1)

            def lanes(t, b):
                dve.wait_ge(counted, t + 1)
                if not isinstance(t, int):
                    dve.wait_ge(stats_done, SIDES * (t + 4))
                nc.vector.scalar_tensor_tensor(out=move[:, b:b + 1], in0=count[:, b:b + 1], scalar=0.5,
                                               in1=to_spare[:, bass.ds(t, 1)], op0=ALU.is_gt, op1=ALU.mult
                                               ).then_inc(moved, 1)
                dve.wait_ge(moved, t + 1)
                nc.vector.tensor_tensor(add_i[:, bass.ds(t, 1)], move[:, b:b + 1], src_f[:, bass.ds(t, 1)],
                                        ALU.add).then_inc(add_ready, 1)

            def message_low(t, b):
                dve.wait_ge(mhi_ready, t + 1)
                nc.vector.scalar_tensor_tensor(out=m_lo[:, b, :], in0=zb[:, b, :], scalar=0.0,
                                               in1=m_hi[:, b, :].bitcast(F32), op0=ALU.max, op1=ALU.subtract
                                               ).then_inc(mlo_ready, 1)

            def step(s, b, pair_slot, first=0, last=TILES - 1):
                def has(d):
                    return not isinstance(s, int) or first <= s + d <= last
                if has(-1):
                    add_bias(s - 1, 1 - b)
                    same_source(s - 1, 1 - b, pair_slot)
                    message_low(s - 1, 1 - b)
                if has(1):
                    low_parts(s + 1, 1 - b)
                if has(2):
                    statistics(s + 2, b)
                if has(-1):
                    lanes(s - 1, 1 - b)
                if has(2):
                    aggregate(s + 2, b)
                    scales(s + 2, b)

            dve.wait_ge(src_loaded, 16)
            dve.wait_ge(spare_made, 1)
            nc.vector.tensor_copy(src_f[:, :], src_i[:, :]).then_inc(src_cast, 1)
            nc.vector.tensor_copy(spare_f[:, :], spare_i[:, :]).then_inc(src_cast, 1)
            dve.wait_ge(src_cast, 2)
            nc.vector.scalar_tensor_tensor(out=to_spare[:, :], in0=src_f[:, :], scalar=-1.0,
                                           in1=spare_f[:, :].to_broadcast([P, TILES]), op0=ALU.mult, op1=ALU.add
                                           ).then_inc(src_cast, 1)
            step(-2, 0, 0)
            for k in range(K):
                dve.wait_ge(w_hi_ready, k + 1)
                nc.vector.tensor_tensor(w_lo[:, k, :], ring[:, k, :], w_hi[:, k, :].bitcast(F32),
                                        ALU.subtract).then_inc(w_lo_ready, 1)
            step(-1, 1, 0)
            dve.wait_ge(bias_loaded, 16)
            dve.wait_ge(consts, 4)
            dve.wait_ge(src_cast, 3)
            for s in range(0, 3):
                step(s, s % 2, (s - 1) // 2 % 2)
            with dve.Fori(3, TILES - 6, 4) as s:
                for d in range(4):
                    step(s + d, (3 + d) % 2, (2 + d) // 2 % 2)
            for s in range(TILES - 3, TILES + 1):
                step(s, s % 2, (s - 1) // 2 % 2)

        @block.scalar
        def _(act):
            def load_row(t, slot):
                act.dma_start(src_row[:, slot, :],
                              src_rows[0:1, bass.ds(t * P, 2 * P)].to_broadcast([P, 2 * P])
                              ).then_inc(row_arrived[slot], 16)

            def high_parts(t, b):
                for s in range(SIDES):
                    act.wait_ge(transposed, SIDES * t + s + 1)
                    if s == 0 and not (isinstance(t, int) and t < 2):
                        act.wait_ge(mm_done, t - 1)
                    nc.scalar.copy(ht_hi[:, b, s, :], ht_ps[b][s][:, :]).then_inc(hi_ready, 1)

            def normalise(t, b):
                act.wait_ge(norm_ready, t + 1)
                if not (isinstance(t, int) and t < 2):
                    act.wait_ge(transposed, SIDES * (t - 1))
                for s in range(SIDES):
                    nc.scalar.activation(h[:, b, s, :], xg[:, b, s, :], ACT.Relu, bias=shift[:, b, s:s + 1],
                                         scale=rstd[:, b, s:s + 1]).then_inc(h_ready, 1)

            def deviation(t, b):
                act.wait_ge(var_ready, SIDES * (t + 1))
                nc.scalar.activation(std[:, b, :], mean_var[:, b, :, 1], ACT.Sqrt, bias=eps[:, :]
                                     ).then_inc(std_ready, 1)

            def message_high(t, b):
                act.wait_ge(biased, t + 1)
                if not (isinstance(t, int) and t < 2):
                    act.wait_ge(agg_done, t - 1)
                nc.scalar.activation(m_hi[:, b, :], zb[:, b, :], ACT.Relu).then_inc(mhi_ready, 1)

            def store_sum(t, b, again):
                act.wait_ge(agg_done, t + 1)
                slot = t
                if again:
                    act.wait_ge(scattered, 16 * (t - RING + 1))
                    slot = t - RING
                nc.scalar.copy(ring[:, bass.ds(slot, 1), :].rearrange("p a o -> p (a o)"), agg_ps[b][:, :]
                               ).then_inc(ring_filled, 1)

            def step(s, b, again=False, row_slot=None):
                def has(d):
                    return not isinstance(s, int) or 0 <= s + d < TILES
                if has(-1):
                    message_high(s - 1, 1 - b)
                if has(-2):
                    store_sum(s - 2, b, again)
                if has(1):
                    high_parts(s + 1, 1 - b)
                if row_slot is not None:
                    act.wait_ge(counted, s - 1)
                    load_row(s + 1, row_slot)
                if has(2):
                    deviation(s + 2, b)
                    normalise(s + 2, b)

            def slot_of(s):
                return (s + 1) // 2 % 2 if s % 2 and 3 <= s <= TILES - 3 else None

            load_row(0, 0)
            load_row(2, 1)
            act.wait_ge(eps_made, 1)
            step(-2, 0)
            act.wait_ge(w_loaded, 16)
            for k in range(K):
                nc.scalar.copy(w_hi[:, k, :], ring[:, k, :]).then_inc(w_hi_ready, 1)
            step(-1, 1)
            for s in range(0, 3):
                step(s, s % 2)
            with act.Fori(3, RING - 1, 4) as s:
                for d in range(4):
                    step(s + d, (3 + d) % 2, row_slot=slot_of(3 + d))
            with act.Fori(RING + 2, TILES - 6, 4) as s:
                for d in range(4):
                    step(s + d, (3 + d) % 2, again=True, row_slot=slot_of(3 + d))
            for s in range(TILES - 3, TILES + 2):
                step(s, s % 2, again=True, row_slot=slot_of(s))

        @block.tensor
        def _(pe):
            def transposes(t, b):
                for s in range(SIDES):
                    pe.wait_ge(h_ready, SIDES * t + s + 1)
                    if not (isinstance(t, int) and t < 2):
                        pe.wait_ge(lo_ready, SIDES * (t - 2) + s + 1)
                    for k in range(KD):
                        last = nc.tensor.transpose(ht_ps[b][s][:, k * P:(k + 1) * P],
                                                   h[:, b, s, k * P:(k + 1) * P], identity[:, :])
                    last.then_inc(transposed, 1)

            def products(t, b):
                if not (isinstance(t, int) and t < 2):
                    pe.wait_ge(biased, t - 1)
                for s in range(SIDES):
                    pe.wait_ge(lo_ready, SIDES * t + s + 1)
                    for k in range(KD):
                        hi = ht_hi[:, b, s, k * P:(k + 1) * P]
                        lo = ht_lo[:, b, s, k * P:(k + 1) * P]
                        c = s * KD + k
                        nc.tensor.matmul(z_ps[b][:, :], hi, w_hi[:, c, :], start=(c == 0), stop=False)
                        nc.tensor.matmul(z_ps[b][:, :], hi, w_lo[:, c, :], start=False, stop=False)
                        last = nc.tensor.matmul(z_ps[b][:, :], lo, w_hi[:, c, :], start=False, stop=(c == K - 1))
                last.then_inc(mm_done, 1)

            def sums(t, b):
                pe.wait_ge(same_ready, t + 1)
                if not (isinstance(t, int) and t < 2):
                    pe.wait_ge(ring_filled, t - 1)
                pe.wait_ge(mlo_ready, t + 1)
                nc.tensor.matmul(agg_ps[b][:, :], same[:, b, :], m_hi[:, b, :], start=True, stop=False)
                nc.tensor.matmul(agg_ps[b][:, :], same[:, b, :], m_lo[:, b, :], start=False, stop=True
                                 ).then_inc(agg_done, 1)

            def step(s, b):
                def has(d):
                    return not isinstance(s, int) or 0 <= s + d < TILES
                if has(1):
                    transposes(s + 1, 1 - b)
                if has(0):
                    products(s, b)
                if has(-1):
                    sums(s - 1, 1 - b)

            pe.wait_ge(consts, 4)
            step(-1, 1)
            pe.wait_ge(w_lo_ready, K)
            step(0, 0)
            step(1, 1)
            step(2, 0)
            with pe.Fori(3, TILES - 6, 4) as s:
                for d in range(4):
                    step(s + d, (3 + d) % 2)
            for s in range(TILES - 3, TILES + 1):
                step(s, s % 2)


def kernel(x, src, dst, L0_gnn_W, L0_gnn_b):
    import numpy as np
    import concourse.bacc as bacc
    from concourse import mybir as mb
    from concourse.bass_utils import run_bass_kernel_spmd

    x, src, dst, w, b = (np.asarray(a) for a in (x, src, dst, L0_gnn_W, L0_gnn_b))
    n, d = x.shape
    edges = src.shape[0]
    tiles = -(-edges // 128)
    pad = tiles * 128 - edges
    src_pad = np.concatenate([src, np.full(pad, n, src.dtype)]).reshape(tiles, 128)
    dst_pad = np.concatenate([dst, np.full(pad, 0, dst.dtype)]).reshape(tiles, 128)
    arrays = {
        "x": np.ascontiguousarray(x),
        "src_cols": np.ascontiguousarray(src_pad.T),
        "src_rows": np.ascontiguousarray(src_pad.reshape(1, -1)),
        "dst_cols": np.ascontiguousarray(dst_pad.T),
        "w_t": np.ascontiguousarray(w.T),
        "bias": np.ascontiguousarray(b.reshape(1, -1)),
    }
    nc = bacc.Bacc("TRN2", target_bir_lowering=False, num_devices=1)
    args = [nc.dram_tensor(name, a.shape, mb.dt.from_np(a.dtype), kind="ExternalInput").ap()
            for name, a in arrays.items()]
    out = nc.dram_tensor("out", (n + 128, d), mb.dt.float32, kind="ExternalOutput").ap()
    gnn_message_passing_kernel(nc, *args, out)
    result = run_bass_kernel_spmd(nc, [arrays], core_ids=[0])
    return result.results[0]["out"][:n]
```

```python
import concourse.bass as bass
from concourse import mybir
from contextlib import ExitStack


def gnn_message_passing_kernel(
    nc: bass.Bass,
    x: bass.AP,
    src_cols: bass.AP,
    src_rows: bass.AP,
    dst_cols: bass.AP,
    w_t: bass.AP,
    bias: bass.AP,
    out: bass.AP,
):
    F32 = mybir.dt.float32
    F32R = mybir.dt.float32r
    I32 = mybir.dt.int32
    ALU = mybir.AluOpType
    ACT = mybir.ActivationFunctionType

    P = 128
    N, D = x.shape
    TILES = src_cols.shape[1]
    OUT = w_t.shape[1]
    SIDES = 2
    KD = D // P
    K = SIDES * KD
    EPS = 1e-5
    PAIRS = TILES // 2
    W_LOADS = 4
    XS = 4
    RING = 56
    FIRST_ADD = RING + 2
    COPY_RUNS = 16
    COPY_ROWS = COPY_RUNS * 25
    COPIES = N // COPY_ROWS
    COPY_SLOTS = 5
    COPY_AHEAD = 3
    assert N % COPY_ROWS == 0 and COPIES % COPY_SLOTS == 0 and TILES % 4 == 2 and RING % 4 == 0 and OUT == D and D == 512
    assert FIRST_ADD <= RING + 4 <= TILES - 8

    ctx = ExitStack()
    with ctx:
        def sb(name, shape, dt):
            return ctx.enter_context(nc.sbuf_tensor(name, shape, dt))

        def ps(name, shape):
            return ctx.enter_context(nc.psum_tensor(name, shape, F32))

        def sem(name):
            return ctx.enter_context(nc.semaphore(name))

        w_hi = sb("w_hi", [P, K, OUT], F32R)
        w_lo = sb("w_lo", [P, K, OUT], F32R)
        bias_bc = sb("bias_bc", [P, OUT], F32)
        src_i = sb("src_i", [P, TILES], I32)
        dst_i = sb("dst_i", [P, TILES], I32)
        src_f = sb("src_f", [P, TILES], F32)
        spare_i = sb("spare_i", [P, 1], I32)
        spare_f = sb("spare_f", [P, 1], F32)
        to_spare = sb("to_spare", [P, TILES], F32)
        identity = sb("identity", [P, P], F32)
        earlier = sb("earlier", [P, 2 * P], F32)
        eps = sb("eps", [P, 1], F32)
        add_i = sb("add_i", [P, TILES], I32)
        xg = sb("xg", [P, XS, SIDES, D], F32)
        stats = sb("stats", [P, 2, SIDES, 6], F32)
        mean_var = sb("mean_var", [P, 2, SIDES, 2], F32)
        std = sb("std", [P, 2, SIDES], F32)
        rstd = sb("rstd", [P, 2, SIDES], F32)
        shift = sb("shift", [P, 2, SIDES], F32)
        h = sb("h", [P, 2, SIDES, D], F32)
        ht_hi = sb("ht_hi", [P, 2, SIDES, KD * P], F32R)
        ht_lo = sb("ht_lo", [P, 2, SIDES, KD * P], F32R)
        src_row = sb("src_row", [P, 2, 2 * P], I32)
        same = sb("same", [P, 3, P], F32R)
        found = sb("found", [P, 2 * P], F32)
        count = sb("count", [P, 2], F32)
        move = sb("move", [P, 2], F32)
        zb = sb("zb", [P, 2, OUT], F32)
        m_hi = sb("m_hi", [P, 2, OUT], F32R)
        m_lo = sb("m_lo", [P, 2, OUT], F32R)
        ring = sb("ring", [P, RING, OUT], F32)

        ht_ps = [[ps(f"ht_ps{b}{s}", [P, KD * P]) for s in range(SIDES)] for b in range(2)]
        z_ps = [ps(f"z_ps{b}", [P, OUT]) for b in range(2)]
        agg_ps = [ps(f"agg_ps{b}", [P, OUT]) for b in range(2)]

        src_loaded = sem("src_loaded")
        dst_loaded = sem("dst_loaded")
        w_loaded = [sem(f"w_loaded{n}") for n in range(W_LOADS)]
        bias_loaded = sem("bias_loaded")
        spare_filled = sem("spare_filled")
        copied = [sem(f"copied{j}") for j in range(COPY_SLOTS)]
        consts = sem("consts")
        eps_made = sem("eps_made")
        spare_made = sem("spare_made")
        x_arrived = [sem(f"x_arrived{b}") for b in range(XS)]
        row_arrived = [sem(f"row_arrived{b}") for b in range(2)]
        scattered = sem("scattered")
        src_cast = sem("src_cast")
        w_hi_ready = sem("w_hi_ready")
        w_lo_ready = sem("w_lo_ready")
        stats_done = sem("stats_done")
        var_ready = sem("var_ready")
        std_ready = sem("std_ready")
        rstd_done = sem("rstd_done")
        norm_ready = sem("norm_ready")
        h_ready = sem("h_ready")
        transposed = sem("transposed")
        hi_ready = sem("hi_ready")
        lo_ready = sem("lo_ready")
        mm_done = sem("mm_done")
        biased = sem("biased")
        mhi_ready = sem("mhi_ready")
        mlo_ready = sem("mlo_ready")
        same_ready = sem("same_ready")
        counted = sem("counted")
        moved = sem("moved")
        add_ready = sem("add_ready")
        agg_done = sem("agg_done")
        ring_filled = sem("ring_filled")

        block = ctx.enter_context(nc.Block())

        @block.sync
        def _(sp):
            sp.dma_start(dst_i[:, :], dst_cols).then_inc(dst_loaded, 16)
            sp.dma_start(src_i[:, :], src_cols).then_inc(src_loaded, 16)
            sp.wait_ge(x_arrived[0], 16 * SIDES)
            w_chunks = w_t.rearrange("(k p) o -> p k o", p=P)
            for n in range(W_LOADS):
                ks = slice(n * K // W_LOADS, (n + 1) * K // W_LOADS)
                sp.dma_start(ring[:, ks, :], w_chunks[:, ks, :]).then_inc(w_loaded[n], 16)
            sp.dma_start(bias_bc[:, :], bias.to_broadcast([P, OUT])).then_inc(bias_loaded, 16)
            sp.dma_start(out[N:N + P, :], x[0:P, :]).then_inc(spare_filled, 16)
            out_runs = out[0:N, :].rearrange("(c a b) d -> c a (b d)", a=COPY_RUNS, c=COPIES)
            x_runs = x.rearrange("(c a b) d -> c a (b d)", a=COPY_RUNS, c=COPIES)
            rounds = COPIES // COPY_SLOTS

            def copy(n, j):
                if j >= COPY_AHEAD:
                    sp.wait_ge(copied[j - COPY_AHEAD], 16 * (n + 1))
                elif not (isinstance(n, int) and n == 0):
                    sp.wait_ge(copied[j - COPY_AHEAD + COPY_SLOTS], 16 * n)
                sp.dma_start(out_runs[COPY_SLOTS * n + j], x_runs[COPY_SLOTS * n + j]).then_inc(copied[j], 16)

            for j in range(COPY_SLOTS):
                copy(0, j)
            with sp.Fori(1, rounds) as n:
                for j in range(COPY_SLOTS):
                    copy(n, j)

        @block.gpsimd
        def _(pool):
            def gather(t):
                b = t % XS
                if t >= XS:
                    pool.wait_ge(h_ready, SIDES * (t - XS + 1))
                for s, (nodes, loaded) in enumerate(((src_i, src_loaded), (dst_i, dst_loaded))):
                    if t == 0:
                        pool.wait_ge(loaded, 16)
                    nc.gpsimd.indirect_dma_start(
                        out=xg[:, b, s, :], out_offset=None, in_=x,
                        in_offset=bass.IndirectOffsetOnAxis(ap=nodes[:, t:t + 1], axis=0),
                        bounds_check=N - 1, oob_is_err=False).then_inc(x_arrived[b], 16)

            def add(pair):
                if pair == 0:
                    pool.wait_ge(spare_filled, 16)
                    for j in range(COPY_SLOTS):
                        pool.wait_ge(copied[j], 16 * (COPIES // COPY_SLOTS))
                else:
                    pool.wait_ge(scattered, 32 * pair)
                pool.wait_ge(add_ready, 2 * pair + 2)
                for t in (2 * pair, 2 * pair + 1):
                    pool.wait_ge(ring_filled, t + 1)
                    nc.gpsimd.indirect_dma_start(
                        out=out, out_offset=bass.IndirectOffsetOnAxis(ap=add_i[:, t:t + 1], axis=0),
                        in_=ring[:, t % RING, :], in_offset=None, bounds_check=N + P - 1,
                        compute_op=ALU.add).then_inc(scattered, 16)

            nc.gpsimd.iota(spare_i[:, :], pattern=[[0, 1]], base=N, channel_multiplier=1).then_inc(spare_made, 1)
            nc.gpsimd.memset(eps[:, :], EPS).then_inc(eps_made, 1)
            nc.gpsimd.memset(identity[:, :], 0.0).then_inc(consts, 1)
            nc.gpsimd.memset(earlier[:, :], 1.0).then_inc(consts, 1)
            pool.wait_ge(consts, 2)
            nc.gpsimd.affine_select(out=identity[:, :], in_=identity[:, :], compare_op=ALU.not_equal, fill=1.0,
                                    base=0, pattern=[[-1, P]], channel_multiplier=1).then_inc(consts, 1)
            nc.gpsimd.affine_select(out=earlier[:, P:2 * P], in_=earlier[:, P:2 * P], compare_op=ALU.is_gt,
                                    fill=0.0, base=0, pattern=[[-1, P]], channel_multiplier=1
                                    ).then_inc(consts, 1)
            for t in range(FIRST_ADD):
                gather(t)
            added = 0
            for t in range(FIRST_ADD, TILES):
                while added < min((t - FIRST_ADD + 1) * 5 // 4, (t - 7) // 2):
                    add(added)
                    added += 1
                gather(t)
            for pair in range(added, PAIRS):
                add(pair)
            pool.wait_ge(scattered, 16 * TILES)

        @block.vector
        def _(dve):
            def statistics(t, m):
                b = m % 2
                dve.wait_ge(x_arrived[m], 8 * (t - m) + 32)
                for s in range(SIDES):
                    nc.vector.bn_stats(stats[:, b, s, :], xg[:, m, s, :]).then_inc(stats_done, 1)

            def aggregate(t, b):
                if isinstance(t, int):
                    dve.wait_ge(stats_done, SIDES * (t + 1))
                for s in range(SIDES):
                    nc.vector.bn_aggr(mean_var[:, b, s, :], stats[:, b, s, :]).then_inc(var_ready, 1)

            def scales(t, b):
                dve.wait_ge(std_ready, t + 1)
                nc.vector.reciprocal(rstd[:, b, :], std[:, b, :]).then_inc(rstd_done, 1)
                dve.wait_ge(rstd_done, t + 1)
                nc.vector.scalar_tensor_tensor(out=shift[:, b, :], in0=mean_var[:, b, :, 0], scalar=-1.0,
                                               in1=rstd[:, b, :], op0=ALU.mult, op1=ALU.mult
                                               ).then_inc(norm_ready, 1)

            def low_parts(t, b):
                for s in range(SIDES):
                    dve.wait_ge(hi_ready, SIDES * t + s + 1)
                    nc.vector.tensor_tensor(ht_lo[:, b, s, :], ht_ps[b][s][:, :], ht_hi[:, b, s, :].bitcast(F32),
                                            ALU.subtract).then_inc(lo_ready, 1)

            def add_bias(t, b):
                dve.wait_ge(mm_done, t + 1)
                if not isinstance(t, int):
                    dve.wait_ge(stats_done, SIDES * (t + 4))
                nc.vector.tensor_tensor(zb[:, b, :], z_ps[b][:, :], bias_bc[:, :], ALU.add).then_inc(biased, 1)

            def same_source(t, m):
                b, row_slot = m % 2, m // 2
                dve.wait_ge(row_arrived[row_slot], 4 * (t - m) + 16)
                if not (isinstance(t, int) and t < 2):
                    dve.wait_ge(agg_done, t - 1)
                width = (b + 1) * P
                row = src_row[:, row_slot, 0:width]
                mine = src_f[:, bass.ds(t, 1)]
                nc.vector.tensor_scalar(same[:, b:2 * b + 1, :].rearrange("p a j -> p (a j)"), row, mine, None,
                                        ALU.is_equal).then_inc(same_ready, 1)
                nc.vector.scalar_tensor_tensor(out=found[:, 0:width], in0=row, scalar=mine,
                                               in1=earlier[:, 2 * P - width:], op0=ALU.is_equal, op1=ALU.mult,
                                               accum_out=count[:, b:b + 1]).then_inc(counted, 1)

            def lanes(t, b):
                dve.wait_ge(counted, t + 1)
                nc.vector.scalar_tensor_tensor(out=move[:, b:b + 1], in0=count[:, b:b + 1], scalar=0.5,
                                               in1=to_spare[:, bass.ds(t, 1)], op0=ALU.is_gt, op1=ALU.mult
                                               ).then_inc(moved, 1)
                dve.wait_ge(moved, t + 1)
                nc.vector.tensor_tensor(add_i[:, bass.ds(t, 1)], move[:, b:b + 1], src_f[:, bass.ds(t, 1)],
                                        ALU.add).then_inc(add_ready, 1)

            def message_low(t, b):
                dve.wait_ge(mhi_ready, t + 1)
                nc.vector.scalar_tensor_tensor(out=m_lo[:, b, :], in0=zb[:, b, :], scalar=0.0,
                                               in1=m_hi[:, b, :].bitcast(F32), op0=ALU.max, op1=ALU.subtract
                                               ).then_inc(mlo_ready, 1)

            def step(s, m):
                b = m % 2

                def has(d):
                    return not isinstance(s, int) or 0 <= s + d < TILES
                if has(2):
                    statistics(s + 2, (m + 2) % 4)
                if has(-1):
                    add_bias(s - 1, 1 - b)
                if has(2):
                    aggregate(s + 2, b)
                if has(-1):
                    same_source(s - 1, (m - 1) % 4)
                if has(2):
                    scales(s + 2, b)
                if has(1):
                    low_parts(s + 1, 1 - b)
                if has(-1):
                    message_low(s - 1, 1 - b)
                    lanes(s - 1, 1 - b)

            dve.wait_ge(src_loaded, 16)
            dve.wait_ge(spare_made, 1)
            nc.vector.tensor_copy(src_f[:, :], src_i[:, :]).then_inc(src_cast, 1)
            nc.vector.tensor_copy(spare_f[:, :], spare_i[:, :]).then_inc(src_cast, 1)
            dve.wait_ge(src_cast, 2)
            nc.vector.scalar_tensor_tensor(out=to_spare[:, :], in0=src_f[:, :], scalar=-1.0,
                                           in1=spare_f[:, :].to_broadcast([P, TILES]), op0=ALU.mult, op1=ALU.add
                                           ).then_inc(src_cast, 1)
            for t in range(2):
                statistics(t, t)
                aggregate(t, t)
                scales(t, t)
            low_parts(0, 0)
            for k in range(K):
                dve.wait_ge(w_hi_ready, k + 1)
                nc.vector.tensor_tensor(w_lo[:, k, :], ring[:, k, :], w_hi[:, k, :].bitcast(F32),
                                        ALU.subtract).then_inc(w_lo_ready, 1)
            dve.wait_ge(bias_loaded, 16)
            dve.wait_ge(consts, 4)
            dve.wait_ge(src_cast, 3)
            for s in range(0, 3):
                step(s, s)
            with dve.Fori(3, TILES - 6, 4) as s:
                for d in range(4):
                    step(s + d, (3 + d) % 4)
            for s in range(TILES - 3, TILES + 1):
                step(s, s % 4)

        @block.scalar
        def _(act):
            def load_row(t, slot):
                act.dma_start(src_row[:, slot, :],
                              src_rows[0:1, bass.ds(t * P, 2 * P)].to_broadcast([P, 2 * P])
                              ).then_inc(row_arrived[slot], 16)

            def high_parts(t, b):
                for s in range(SIDES):
                    act.wait_ge(transposed, SIDES * t + s + 1)
                    if s == 0 and not (isinstance(t, int) and t < 2):
                        act.wait_ge(mm_done, t - 1)
                    nc.scalar.copy(ht_hi[:, b, s, :], ht_ps[b][s][:, :]).then_inc(hi_ready, 1)

            def normalise(t, m):
                b = m % 2
                act.wait_ge(norm_ready, t + 1)
                if not (isinstance(t, int) and t < 2):
                    act.wait_ge(transposed, SIDES * (t - 1))
                for s in range(SIDES):
                    nc.scalar.activation(h[:, b, s, :], xg[:, m, s, :], ACT.Relu, bias=shift[:, b, s:s + 1],
                                         scale=rstd[:, b, s:s + 1]).then_inc(h_ready, 1)

            def deviation(t, b):
                act.wait_ge(var_ready, SIDES * (t + 1))
                nc.scalar.activation(std[:, b, :], mean_var[:, b, :, 1], ACT.Sqrt, bias=eps[:, :]
                                     ).then_inc(std_ready, 1)

            def message_high(t, b):
                act.wait_ge(biased, t + 1)
                if not (isinstance(t, int) and t < 2):
                    act.wait_ge(agg_done, t - 1)
                nc.scalar.activation(m_hi[:, b, :], zb[:, b, :], ACT.Relu).then_inc(mhi_ready, 1)

            def store_sums(t, again):
                if again:
                    act.wait_ge(scattered, 16 * (t - RING) + 32)
                for b in range(2):
                    act.wait_ge(agg_done, t + b + 1)
                    slot = t + b - RING if again else t + b
                    nc.scalar.copy(ring[:, bass.ds(slot, 1), :].rearrange("p a o -> p (a o)"), agg_ps[b][:, :]
                                   ).then_inc(ring_filled, 1)

            def step(s, m, again=False):
                b = m % 2

                def has(d):
                    return not isinstance(s, int) or 0 <= s + d < TILES
                if has(1):
                    high_parts(s + 1, 1 - b)
                if has(-1):
                    message_high(s - 1, 1 - b)
                if has(2):
                    deviation(s + 2, b)
                if b and has(-3):
                    store_sums(s - 3, again)
                if b and has(-2) and has(2):
                    act.wait_ge(counted, s - 1)
                    load_row(s + 1, (m + 1) // 2 % 2)
                if has(2):
                    normalise(s + 2, (m + 2) % 4)

            load_row(0, 0)
            load_row(2, 1)
            act.wait_ge(eps_made, 1)
            for t in range(2):
                deviation(t, t)
                normalise(t, t)
            high_parts(0, 0)
            for k in range(K):
                if k % (K // W_LOADS) == 0:
                    act.wait_ge(w_loaded[k // (K // W_LOADS)], 16)
                nc.scalar.copy(w_hi[:, k, :], ring[:, k, :]).then_inc(w_hi_ready, 1)
            for s in range(0, 3):
                step(s, s)
            with act.Fori(3, RING, 4) as s:
                for d in range(4):
                    step(s + d, (3 + d) % 4)
            with act.Fori(RING + 3, TILES - 6, 4) as s:
                for d in range(4):
                    step(s + d, (3 + d) % 4, again=True)
            for s in range(TILES - 3, TILES + 2):
                step(s, s % 4, again=True)

        @block.tensor
        def _(pe):
            def transposes(t, b):
                for s in range(SIDES):
                    pe.wait_ge(h_ready, SIDES * t + s + 1)
                    if not (isinstance(t, int) and t < 2):
                        pe.wait_ge(lo_ready, SIDES * (t - 2) + s + 1)
                    for k in range(KD):
                        last = nc.tensor.transpose(ht_ps[b][s][:, k * P:(k + 1) * P],
                                                   h[:, b, s, k * P:(k + 1) * P], identity[:, :])
                    last.then_inc(transposed, 1)

            def products(t, b):
                if not (isinstance(t, int) and t < 2):
                    pe.wait_ge(biased, t - 1)
                for s in range(SIDES):
                    pe.wait_ge(lo_ready, SIDES * t + s + 1)
                    for k in range(KD):
                        if isinstance(t, int) and t == 0:
                            pe.wait_ge(w_lo_ready, s * KD + k + 1)
                        hi = ht_hi[:, b, s, k * P:(k + 1) * P]
                        lo = ht_lo[:, b, s, k * P:(k + 1) * P]
                        c = s * KD + k
                        nc.tensor.matmul(z_ps[b][:, :], hi, w_hi[:, c, :], start=(c == 0), stop=False)
                        nc.tensor.matmul(z_ps[b][:, :], hi, w_lo[:, c, :], start=False, stop=False)
                        last = nc.tensor.matmul(z_ps[b][:, :], lo, w_hi[:, c, :], start=False, stop=(c == K - 1))
                last.then_inc(mm_done, 1)

            def sums(t):
                pe.wait_ge(same_ready, t + 2)
                if not isinstance(t, int) or t >= 2:
                    pe.wait_ge(ring_filled, t)
                pe.wait_ge(mlo_ready, t + 2)
                nc.tensor.matmul(agg_ps[0][:, :], same[:, 0, :], m_hi[:, 0, :], start=True, stop=False)
                nc.tensor.matmul(agg_ps[0][:, :], same[:, 0, :], m_lo[:, 0, :], start=False, stop=False)
                nc.tensor.matmul(agg_ps[0][:, :], same[:, 1, :], m_hi[:, 1, :], start=False, stop=False)
                nc.tensor.matmul(agg_ps[0][:, :], same[:, 1, :], m_lo[:, 1, :], start=False, stop=True
                                 ).then_inc(agg_done, 1)
                nc.tensor.matmul(agg_ps[1][:, :], same[:, 2, :], m_hi[:, 1, :], start=True, stop=False)
                nc.tensor.matmul(agg_ps[1][:, :], same[:, 2, :], m_lo[:, 1, :], start=False, stop=True
                                 ).then_inc(agg_done, 1)

            def step(s, b):
                def has(d):
                    return not isinstance(s, int) or 0 <= s + d < TILES
                if has(1):
                    transposes(s + 1, 1 - b)
                if has(0):
                    products(s, b)
                if not b and has(-2):
                    sums(s - 2)

            pe.wait_ge(consts, 4)
            step(-1, 1)
            for s in range(0, 3):
                step(s, s % 2)
            with pe.Fori(3, TILES - 4, 2) as s:
                for d in range(2):
                    step(s + d, (3 + d) % 2)
            for s in range(TILES - 3, TILES + 1):
                step(s, s % 2)


def kernel(x, src, dst, L0_gnn_W, L0_gnn_b):
    import numpy as np
    import concourse.bacc as bacc
    from concourse import mybir as mb
    from concourse.bass_utils import run_bass_kernel_spmd

    x, src, dst, w, b = (np.asarray(a) for a in (x, src, dst, L0_gnn_W, L0_gnn_b))
    n, d = x.shape
    edges = src.shape[0]
    tiles = -(-edges // 128)
    pad = tiles * 128 - edges
    src_pad = np.concatenate([src, np.full(pad, n, src.dtype)]).reshape(tiles, 128)
    dst_pad = np.concatenate([dst, np.full(pad, 0, dst.dtype)]).reshape(tiles, 128)
    arrays = {
        "x": np.ascontiguousarray(x),
        "src_cols": np.ascontiguousarray(src_pad.T),
        "src_rows": np.ascontiguousarray(src_pad.reshape(1, -1)),
        "dst_cols": np.ascontiguousarray(dst_pad.T),
        "w_t": np.ascontiguousarray(w.T),
        "bias": np.ascontiguousarray(b.reshape(1, -1)),
    }
    nc = bacc.Bacc("TRN2", target_bir_lowering=False, num_devices=1)
    args = [nc.dram_tensor(name, a.shape, mb.dt.from_np(a.dtype), kind="ExternalInput").ap()
            for name, a in arrays.items()]
    out = nc.dram_tensor("out", (n + 128, d), mb.dt.float32, kind="ExternalOutput").ap()
    gnn_message_passing_kernel(nc, *args, out)
    result = run_bass_kernel_spmd(nc, [arrays], core_ids=[0])
    return result.results[0]["out"][:n]
```

```python
import concourse.bass as bass
from concourse import mybir
from contextlib import ExitStack


def gnn_message_passing_kernel(
    nc: bass.Bass,
    x: bass.AP,
    src_cols: bass.AP,
    src_rows: bass.AP,
    dst_cols: bass.AP,
    w_t: bass.AP,
    bias: bass.AP,
    out: bass.AP,
):
    F32 = mybir.dt.float32
    F32R = mybir.dt.float32r
    I32 = mybir.dt.int32
    ALU = mybir.AluOpType
    ACT = mybir.ActivationFunctionType

    P = 128
    N, D = x.shape
    TILES = src_cols.shape[1]
    OUT = w_t.shape[1]
    SIDES = 2
    KD = D // P
    K = SIDES * KD
    EPS = 1e-5
    PAIRS = TILES // 2
    W_LOADS = 4
    W_FIRST = 2
    XS = 4
    RING = 60
    FIRST_ADD = RING
    COPY_RUNS = 16
    COPY_ROWS = COPY_RUNS * 25
    COPIES = N // COPY_ROWS
    COPY_SLOTS = 5
    COPY_AHEAD = 4
    assert N % COPY_ROWS == 0 and COPIES % COPY_SLOTS == 0 and TILES % 4 == 2 and RING % 4 == 0 and OUT == D and D == 512
    assert FIRST_ADD <= RING + 4 <= TILES - 8

    ctx = ExitStack()
    with ctx:
        def sb(name, shape, dt):
            return ctx.enter_context(nc.sbuf_tensor(name, shape, dt))

        def ps(name, shape):
            return ctx.enter_context(nc.psum_tensor(name, shape, F32))

        def sem(name):
            return ctx.enter_context(nc.semaphore(name))

        w_hi = sb("w_hi", [P, K, OUT], F32R)
        w_lo = sb("w_lo", [P, K, OUT], F32R)
        bias_bc = sb("bias_bc", [P, OUT], F32)
        src_i = sb("src_i", [P, TILES], I32)
        dst_i = sb("dst_i", [P, TILES], I32)
        src_f = sb("src_f", [P, TILES], F32)
        spare_i = sb("spare_i", [P, 2], I32)
        spare_f = sb("spare_f", [P, 2], F32)
        to_spare = sb("to_spare", [P, TILES], F32)
        identity = sb("identity", [P, P], F32)
        earlier = sb("earlier", [P, 2 * P], F32)
        eps = sb("eps", [P, 1], F32)
        warm = sb("warm", [P, 1], F32)
        add_i = sb("add_i", [P, TILES], I32)
        xg = sb("xg", [P, XS, SIDES, D], F32)
        stats = sb("stats", [P, 2, SIDES, 6], F32)
        mean_var = sb("mean_var", [P, 2, SIDES, 2], F32)
        std = sb("std", [P, 2, SIDES], F32)
        rough = sb("rough", [P, 2, SIDES], F32)
        newton = sb("newton", [P, 2, 3, SIDES], F32)
        rstd = sb("rstd", [P, 2, SIDES], F32)
        neg_mean = sb("neg_mean", [P, 2, SIDES], F32)
        h = sb("h", [P, 2, SIDES, D], F32)
        ht_hi = sb("ht_hi", [P, 2, SIDES, KD * P], F32R)
        ht_lo = sb("ht_lo", [P, 2, SIDES, KD * P], F32R)
        src_row = sb("src_row", [P, 2, 2 * P], I32)
        same = sb("same", [P, 3, P], F32R)
        found = sb("found", [P, 2 * P], F32)
        count = sb("count", [P, 2], F32)
        move = sb("move", [P, 2], F32)
        zb = sb("zb", [P, 2, OUT], F32)
        m_hi = sb("m_hi", [P, 2, OUT], F32R)
        m_lo = sb("m_lo", [P, 2, OUT], F32R)
        ring = sb("ring", [P, RING, OUT], F32)

        ht_ps = [[ps(f"ht_ps{b}{s}", [P, KD * P]) for s in range(SIDES)] for b in range(2)]
        z_ps = [ps(f"z_ps{b}", [P, OUT]) for b in range(2)]
        agg_ps = [ps(f"agg_ps{b}", [P, OUT]) for b in range(2)]

        src_loaded = sem("src_loaded")
        dst_loaded = sem("dst_loaded")
        w_loaded = [sem(f"w_loaded{n}") for n in range(W_LOADS)]
        bias_loaded = sem("bias_loaded")
        spare_filled = sem("spare_filled")
        copied = [sem(f"copied{j}") for j in range(COPY_SLOTS)]
        consts = sem("consts")
        eps_made = sem("eps_made")
        spare_made = sem("spare_made")
        x_arrived = [sem(f"x_arrived{b}") for b in range(XS)]
        row_arrived = [sem(f"row_arrived{b}") for b in range(2)]
        scattered = sem("scattered")
        src_cast = sem("src_cast")
        w_hi_ready = sem("w_hi_ready")
        w_lo_ready = sem("w_lo_ready")
        stats_done = sem("stats_done")
        var_ready = sem("var_ready")
        std_ready = sem("std_ready")
        rstd_done = sem("rstd_done")
        mean_ready = sem("mean_ready")
        centred = sem("centred")
        h_ready = sem("h_ready")
        transposed = sem("transposed")
        hi_ready = sem("hi_ready")
        lo_ready = sem("lo_ready")
        mm_done = sem("mm_done")
        biased = sem("biased")
        mhi_ready = sem("mhi_ready")
        mlo_ready = sem("mlo_ready")
        same_ready = sem("same_ready")
        counted = sem("counted")
        moved = sem("moved")
        add_ready = sem("add_ready")
        agg_done = sem("agg_done")
        ring_filled = sem("ring_filled")

        block = ctx.enter_context(nc.Block())

        @block.sync
        def _(sp):
            sp.dma_start(dst_i[:, :], dst_cols).then_inc(dst_loaded, 16)
            sp.dma_start(src_i[:, :], src_cols).then_inc(src_loaded, 16)
            w_chunks = w_t.rearrange("(k p) o -> p k o", p=P)
            for n in range(W_LOADS):
                if n == 1:
                    sp.wait_ge(x_arrived[0], 16 * SIDES)
                ks = slice(n * K // W_LOADS, (n + 1) * K // W_LOADS)
                sp.dma_start(ring[:, ks, :], w_chunks[:, ks, :]).then_inc(w_loaded[n], 16)
            sp.dma_start(bias_bc[:, :], bias.to_broadcast([P, OUT])).then_inc(bias_loaded, 16)
            sp.dma_start(out[N:N + 2 * P, :], x[0:2 * P, :]).then_inc(spare_filled, 16)
            out_runs = out[0:N, :].rearrange("(c a b) d -> c a (b d)", a=COPY_RUNS, c=COPIES)
            x_runs = x.rearrange("(c a b) d -> c a (b d)", a=COPY_RUNS, c=COPIES)
            rounds = COPIES // COPY_SLOTS

            def copy(n, j):
                if j >= COPY_AHEAD:
                    sp.wait_ge(copied[j - COPY_AHEAD], 16 * (n + 1))
                elif not (isinstance(n, int) and n == 0):
                    sp.wait_ge(copied[j - COPY_AHEAD + COPY_SLOTS], 16 * n)
                sp.dma_start(out_runs[COPY_SLOTS * n + j], x_runs[COPY_SLOTS * n + j]).then_inc(copied[j], 16)

            for j in range(COPY_SLOTS):
                copy(0, j)
            with sp.Fori(1, rounds) as n:
                for j in range(COPY_SLOTS):
                    copy(n, j)

        @block.gpsimd
        def _(pool):
            def gather(t):
                b = t % XS
                if t >= XS:
                    pool.wait_ge(centred, SIDES * (t - XS + 1))
                for s, (nodes, loaded) in enumerate(((src_i, src_loaded), (dst_i, dst_loaded))):
                    if t == 0:
                        pool.wait_ge(loaded, 16)
                    nc.gpsimd.indirect_dma_start(
                        out=xg[:, b, s, :], out_offset=None, in_=x,
                        in_offset=bass.IndirectOffsetOnAxis(ap=nodes[:, t:t + 1], axis=0),
                        bounds_check=N - 1, oob_is_err=False).then_inc(x_arrived[b], 16)

            def add(pair):
                if pair == 0:
                    pool.wait_ge(spare_filled, 16)
                    for j in range(COPY_SLOTS):
                        pool.wait_ge(copied[j], 16 * (COPIES // COPY_SLOTS))
                else:
                    pool.wait_ge(scattered, 32 * pair)
                pool.wait_ge(add_ready, 2 * pair + 2)
                for t in (2 * pair, 2 * pair + 1):
                    pool.wait_ge(ring_filled, t + 1)
                    nc.gpsimd.indirect_dma_start(
                        out=out, out_offset=bass.IndirectOffsetOnAxis(ap=add_i[:, t:t + 1], axis=0),
                        in_=ring[:, t % RING, :], in_offset=None, bounds_check=N + 2 * P - 1,
                        compute_op=ALU.add).then_inc(scattered, 16)

            nc.gpsimd.iota(spare_i[:, :], pattern=[[P, 2]], base=N, channel_multiplier=1).then_inc(spare_made, 1)
            nc.gpsimd.memset(eps[:, :], EPS).then_inc(eps_made, 1)
            nc.gpsimd.memset(identity[:, :], 0.0).then_inc(consts, 1)
            nc.gpsimd.memset(earlier[:, :], 1.0).then_inc(consts, 1)
            pool.wait_ge(consts, 2)
            nc.gpsimd.affine_select(out=identity[:, :], in_=identity[:, :], compare_op=ALU.not_equal, fill=1.0,
                                    base=0, pattern=[[-1, P]], channel_multiplier=1).then_inc(consts, 1)
            nc.gpsimd.affine_select(out=earlier[:, P:2 * P], in_=earlier[:, P:2 * P], compare_op=ALU.is_gt,
                                    fill=0.0, base=0, pattern=[[-1, P]], channel_multiplier=1
                                    ).then_inc(consts, 1)
            for t in range(FIRST_ADD):
                gather(t)
            added = 0
            for t in range(FIRST_ADD, TILES):
                while added < min((t - FIRST_ADD + 1) * 5 // 4, (t - 7) // 2):
                    add(added)
                    added += 1
                gather(t)
            for pair in range(added, PAIRS):
                add(pair)
            pool.wait_ge(scattered, 16 * TILES)

        @block.vector
        def _(dve):
            def statistics(t, m):
                b = m % 2
                dve.wait_ge(x_arrived[m], 8 * (t - m) + 32)
                for s in range(SIDES):
                    nc.vector.bn_stats(stats[:, b, s, :], xg[:, m, s, :]).then_inc(stats_done, 1)

            def aggregate(t, b):
                if isinstance(t, int):
                    dve.wait_ge(stats_done, SIDES * (t + 1))
                for s in range(SIDES):
                    nc.vector.bn_aggr(mean_var[:, b, s, :], stats[:, b, s, :]).then_inc(var_ready, 1)
                dve.wait_ge(var_ready, SIDES * (t + 1))
                nc.vector.tensor_scalar(neg_mean[:, b, :], mean_var[:, b, :, 0], -1.0, None, ALU.mult
                                        ).then_inc(mean_ready, 1)

            def scales(t, b):
                dve.wait_ge(std_ready, t + 1)
                nc.vector.reciprocal(rough[:, b, :], std[:, b, :]).then_inc(rstd_done, 1)
                dve.wait_ge(rstd_done, 5 * t + 1)
                nc.vector.scalar_tensor_tensor(out=newton[:, b, 0, :], in0=mean_var[:, b, :, 1], scalar=EPS,
                                               in1=rough[:, b, :], op0=ALU.add, op1=ALU.mult
                                               ).then_inc(rstd_done, 1)
                dve.wait_ge(rstd_done, 5 * t + 2)
                nc.vector.tensor_tensor(newton[:, b, 1, :], newton[:, b, 0, :], rough[:, b, :], ALU.mult
                                        ).then_inc(rstd_done, 1)
                dve.wait_ge(rstd_done, 5 * t + 3)
                nc.vector.tensor_scalar(newton[:, b, 2, :], newton[:, b, 1, :], -0.5, 1.5, ALU.mult, ALU.add
                                        ).then_inc(rstd_done, 1)
                dve.wait_ge(rstd_done, 5 * t + 4)
                nc.vector.tensor_tensor(rstd[:, b, :], newton[:, b, 2, :], rough[:, b, :], ALU.mult
                                        ).then_inc(rstd_done, 1)

            def low_parts(t, b):
                for s in range(SIDES):
                    dve.wait_ge(hi_ready, SIDES * t + s + 1)
                    nc.vector.tensor_tensor(ht_lo[:, b, s, :], ht_ps[b][s][:, :], ht_hi[:, b, s, :].bitcast(F32),
                                            ALU.subtract).then_inc(lo_ready, 1)

            def add_bias(t, b):
                dve.wait_ge(mm_done, t + 1)
                if not isinstance(t, int):
                    dve.wait_ge(stats_done, SIDES * (t + 4))
                nc.vector.tensor_tensor(zb[:, b, :], z_ps[b][:, :], bias_bc[:, :], ALU.add).then_inc(biased, 1)

            def same_source(t, m):
                b, row_slot = m % 2, m // 2
                dve.wait_ge(row_arrived[row_slot], 4 * (t - m) + 16)
                if not (isinstance(t, int) and t < 2):
                    dve.wait_ge(agg_done, t - 1)
                width = (b + 1) * P
                row = src_row[:, row_slot, 0:width]
                mine = src_f[:, bass.ds(t, 1)]
                nc.vector.tensor_scalar(same[:, b:2 * b + 1, :].rearrange("p a j -> p (a j)"), row, mine, None,
                                        ALU.is_equal).then_inc(same_ready, 1)
                nc.vector.scalar_tensor_tensor(out=found[:, 0:width], in0=row, scalar=mine,
                                               in1=earlier[:, 2 * P - width:], op0=ALU.is_equal, op1=ALU.mult,
                                               accum_out=count[:, b:b + 1]).then_inc(counted, 1)

            def lanes(t, b):
                dve.wait_ge(counted, t + 1)
                nc.vector.scalar_tensor_tensor(out=move[:, b:b + 1], in0=count[:, b:b + 1], scalar=0.5,
                                               in1=to_spare[:, bass.ds(t, 1)], op0=ALU.is_gt, op1=ALU.mult
                                               ).then_inc(moved, 1)
                dve.wait_ge(moved, t + 1)
                nc.vector.tensor_tensor(add_i[:, bass.ds(t, 1)], move[:, b:b + 1], src_f[:, bass.ds(t, 1)],
                                        ALU.add).then_inc(add_ready, 1)

            def message_low(t, b):
                dve.wait_ge(mhi_ready, t + 1)
                nc.vector.scalar_tensor_tensor(out=m_lo[:, b, :], in0=zb[:, b, :], scalar=0.0,
                                               in1=m_hi[:, b, :].bitcast(F32), op0=ALU.max, op1=ALU.subtract
                                               ).then_inc(mlo_ready, 1)

            def step(s, m):
                b = m % 2

                def has(d):
                    return not isinstance(s, int) or 0 <= s + d < TILES
                if has(2):
                    statistics(s + 2, (m + 2) % 4)
                if has(-1):
                    add_bias(s - 1, 1 - b)
                if has(2):
                    aggregate(s + 2, b)
                if has(-1):
                    same_source(s - 1, (m - 1) % 4)
                if has(2):
                    scales(s + 2, b)
                if has(1):
                    low_parts(s + 1, 1 - b)
                if has(-1):
                    message_low(s - 1, 1 - b)
                    lanes(s - 1, 1 - b)

            dve.wait_ge(src_loaded, 16)
            dve.wait_ge(spare_made, 1)
            nc.vector.tensor_copy(src_f[:, :], src_i[:, :]).then_inc(src_cast, 1)
            nc.vector.tensor_copy(spare_f[:, :], spare_i[:, :]).then_inc(src_cast, 1)
            dve.wait_ge(src_cast, 2)
            for b in range(2):
                nc.vector.scalar_tensor_tensor(out=to_spare[:, b::2], in0=src_f[:, b::2], scalar=-1.0,
                                               in1=spare_f[:, b:b + 1].to_broadcast([P, PAIRS]),
                                               op0=ALU.mult, op1=ALU.add).then_inc(src_cast, 1)
            def w_low_parts(first, end):
                for k in range(first, end):
                    dve.wait_ge(w_hi_ready, k + 1)
                    nc.vector.tensor_tensor(w_lo[:, k, :], ring[:, k, :], w_hi[:, k, :].bitcast(F32),
                                            ALU.subtract).then_inc(w_lo_ready, 1)

            w_low_parts(0, W_FIRST)
            statistics(0, 0)
            aggregate(0, 0)
            scales(0, 0)
            statistics(1, 1)
            aggregate(1, 1)
            w_low_parts(W_FIRST, KD)
            low_parts(0, 0)
            w_low_parts(KD, K)
            scales(1, 1)
            dve.wait_ge(bias_loaded, 16)
            dve.wait_ge(consts, 4)
            dve.wait_ge(src_cast, 4)
            for s in range(0, 3):
                step(s, s)
            with dve.Fori(3, TILES - 6, 4) as s:
                for d in range(4):
                    step(s + d, (3 + d) % 4)
            for s in range(TILES - 3, TILES + 1):
                step(s, s % 4)

        @block.scalar
        def _(act):
            def load_row(t, slot):
                act.dma_start(src_row[:, slot, :],
                              src_rows[0:1, bass.ds(t * P, 2 * P)].to_broadcast([P, 2 * P])
                              ).then_inc(row_arrived[slot], 16)

            def w_high_parts(first, end):
                for k in range(first, end):
                    if k % (K // W_LOADS) == 0:
                        act.wait_ge(w_loaded[k // (K // W_LOADS)], 16)
                    nc.scalar.copy(w_hi[:, k, :], ring[:, k, :]).then_inc(w_hi_ready, 1)

            def high_parts(t, b):
                for s in range(SIDES):
                    act.wait_ge(transposed, SIDES * t + s + 1)
                    if s == 0 and not (isinstance(t, int) and t < 2):
                        act.wait_ge(mm_done, t - 1)
                    nc.scalar.copy(ht_hi[:, b, s, :], ht_ps[b][s][:, :]).then_inc(hi_ready, 1)

            def centre(t, m):
                b = m % 2
                act.wait_ge(mean_ready, t + 1)
                if not (isinstance(t, int) and t < 2):
                    act.wait_ge(transposed, SIDES * (t - 1))
                for s in range(SIDES):
                    nc.scalar.activation(h[:, b, s, :], xg[:, m, s, :], ACT.Relu, bias=neg_mean[:, b, s:s + 1]
                                         ).then_inc(centred, 1)

            def divide(t, b):
                act.wait_ge(rstd_done, 5 * (t + 1))
                for s in range(SIDES):
                    act.wait_ge(centred, SIDES * t + s + 1)
                    nc.scalar.activation(h[:, b, s, :], h[:, b, s, :], ACT.Copy, scale=rstd[:, b, s:s + 1]
                                         ).then_inc(h_ready, 1)

            def deviation(t, b):
                act.wait_ge(var_ready, SIDES * (t + 1))
                nc.scalar.activation(std[:, b, :], mean_var[:, b, :, 1], ACT.Sqrt, bias=eps[:, :]
                                     ).then_inc(std_ready, 1)

            def message_high(t, b):
                act.wait_ge(biased, t + 1)
                if not (isinstance(t, int) and t < 2):
                    act.wait_ge(agg_done, t - 1)
                nc.scalar.activation(m_hi[:, b, :], zb[:, b, :], ACT.Relu).then_inc(mhi_ready, 1)

            def store_sums(t, again):
                if again:
                    act.wait_ge(scattered, 16 * (t - RING) + 32)
                for b in range(2):
                    act.wait_ge(agg_done, t + b + 1)
                    slot = t + b - RING if again else t + b
                    nc.scalar.copy(ring[:, bass.ds(slot, 1), :].rearrange("p a o -> p (a o)"), agg_ps[b][:, :]
                                   ).then_inc(ring_filled, 1)

            def step(s, m, again=False):
                b = m % 2

                def has(d):
                    return not isinstance(s, int) or 0 <= s + d < TILES
                if has(1):
                    high_parts(s + 1, 1 - b)
                if has(-1):
                    message_high(s - 1, 1 - b)
                if has(2):
                    deviation(s + 2, b)
                    centre(s + 2, (m + 2) % 4)
                if b and has(-3):
                    store_sums(s - 3, again)
                if b and has(-2) and has(2):
                    act.wait_ge(counted, s - 1)
                    load_row(s + 1, (m + 1) // 2 % 2)
                if has(2):
                    divide(s + 2, b)

            load_row(0, 0)
            load_row(2, 1)
            act.wait_ge(eps_made, 1)
            nc.scalar.activation(warm[:, :], eps[:, :], ACT.Sqrt)
            w_high_parts(0, W_FIRST)
            deviation(0, 0)
            centre(0, 0)
            divide(0, 0)
            w_high_parts(W_FIRST, KD)
            high_parts(0, 0)
            w_high_parts(KD, K)
            deviation(1, 1)
            centre(1, 1)
            divide(1, 1)
            for s in range(0, 3):
                step(s, s)
            with act.Fori(3, RING, 4) as s:
                for d in range(4):
                    step(s + d, (3 + d) % 4)
            with act.Fori(RING + 3, TILES - 6, 4) as s:
                for d in range(4):
                    step(s + d, (3 + d) % 4, again=True)
            for s in range(TILES - 3, TILES + 2):
                step(s, s % 4, again=True)

        @block.tensor
        def _(pe):
            def transposes(t, b):
                for s in range(SIDES):
                    pe.wait_ge(h_ready, SIDES * t + s + 1)
                    if not (isinstance(t, int) and t < 2):
                        pe.wait_ge(lo_ready, SIDES * (t - 2) + s + 1)
                    for k in range(KD):
                        last = nc.tensor.transpose(ht_ps[b][s][:, k * P:(k + 1) * P],
                                                   h[:, b, s, k * P:(k + 1) * P], identity[:, :])
                    last.then_inc(transposed, 1)

            def products(t, b):
                if not (isinstance(t, int) and t < 2):
                    pe.wait_ge(biased, t - 1)
                for s in range(SIDES):
                    pe.wait_ge(lo_ready, SIDES * t + s + 1)
                    for k in range(KD):
                        if isinstance(t, int) and t == 0:
                            pe.wait_ge(w_lo_ready, s * KD + k + 1)
                        hi = ht_hi[:, b, s, k * P:(k + 1) * P]
                        lo = ht_lo[:, b, s, k * P:(k + 1) * P]
                        c = s * KD + k
                        nc.tensor.matmul(z_ps[b][:, :], hi, w_hi[:, c, :], start=(c == 0), stop=False)
                        nc.tensor.matmul(z_ps[b][:, :], hi, w_lo[:, c, :], start=False, stop=False)
                        last = nc.tensor.matmul(z_ps[b][:, :], lo, w_hi[:, c, :], start=False, stop=(c == K - 1))
                last.then_inc(mm_done, 1)

            def sums(t):
                pe.wait_ge(same_ready, t + 2)
                if not isinstance(t, int) or t >= 2:
                    pe.wait_ge(ring_filled, t)
                pe.wait_ge(mlo_ready, t + 2)
                nc.tensor.matmul(agg_ps[0][:, :], same[:, 0, :], m_hi[:, 0, :], start=True, stop=False)
                nc.tensor.matmul(agg_ps[0][:, :], same[:, 0, :], m_lo[:, 0, :], start=False, stop=False)
                nc.tensor.matmul(agg_ps[0][:, :], same[:, 1, :], m_hi[:, 1, :], start=False, stop=False)
                nc.tensor.matmul(agg_ps[0][:, :], same[:, 1, :], m_lo[:, 1, :], start=False, stop=True
                                 ).then_inc(agg_done, 1)
                nc.tensor.matmul(agg_ps[1][:, :], same[:, 2, :], m_hi[:, 1, :], start=True, stop=False)
                nc.tensor.matmul(agg_ps[1][:, :], same[:, 2, :], m_lo[:, 1, :], start=False, stop=True
                                 ).then_inc(agg_done, 1)

            def step(s, b):
                def has(d):
                    return not isinstance(s, int) or 0 <= s + d < TILES
                if has(1):
                    transposes(s + 1, 1 - b)
                if has(0):
                    products(s, b)
                if not b and has(-2):
                    sums(s - 2)

            pe.wait_ge(consts, 4)
            transposes(0, 0)
            products(0, 0)
            transposes(1, 1)
            for s in range(1, 3):
                step(s, s % 2)
            with pe.Fori(3, TILES - 4, 2) as s:
                for d in range(2):
                    step(s + d, (3 + d) % 2)
            for s in range(TILES - 3, TILES + 1):
                step(s, s % 2)


def kernel(x, src, dst, L0_gnn_W, L0_gnn_b):
    import numpy as np
    import concourse.bacc as bacc
    from concourse import mybir as mb
    from concourse.bass_utils import run_bass_kernel_spmd

    x, src, dst, w, b = (np.asarray(a) for a in (x, src, dst, L0_gnn_W, L0_gnn_b))
    n, d = x.shape
    edges = src.shape[0]
    tiles = -(-edges // 128)
    pad = tiles * 128 - edges
    src_pad = np.concatenate([src, np.full(pad, n, src.dtype)]).reshape(tiles, 128)
    dst_pad = np.concatenate([dst, np.full(pad, 0, dst.dtype)]).reshape(tiles, 128)
    arrays = {
        "x": np.ascontiguousarray(x),
        "src_cols": np.ascontiguousarray(src_pad.T),
        "src_rows": np.ascontiguousarray(src_pad.reshape(1, -1)),
        "dst_cols": np.ascontiguousarray(dst_pad.T),
        "w_t": np.ascontiguousarray(w.T),
        "bias": np.ascontiguousarray(b.reshape(1, -1)),
    }
    nc = bacc.Bacc("TRN2", target_bir_lowering=False, num_devices=1, dynamic_dma_scratch_size=8192)
    args = [nc.dram_tensor(name, a.shape, mb.dt.from_np(a.dtype), kind="ExternalInput").ap()
            for name, a in arrays.items()]
    out = nc.dram_tensor("out", (n + 256, d), mb.dt.float32, kind="ExternalOutput").ap()
    gnn_message_passing_kernel(nc, *args, out)
    result = run_bass_kernel_spmd(nc, [arrays], core_ids=[0])
    return result.results[0]["out"][:n]
```
